# Optimizing a Trainium2 kernel written in Bass

```python
import numpy as np
import jax
import jax.numpy as jnp

def _softmax(x, axis=-1):
    return jax.nn.softmax(x, axis=axis)

def _gelu(x):
    return jax.nn.gelu(x, approximate=True)

def _silu(x):
    return jax.nn.silu(x)

def _sigmoid(x):
    return jax.nn.sigmoid(x)

def _layernorm(x, axis=-1, eps=1e-05):
    m = jnp.mean(x, axis=axis, keepdims=True)
    v = jnp.var(x, axis=axis, keepdims=True)
    return (x - m) / jnp.sqrt(v + eps)

def _scatter_add(tgt, idx, src, axis=0):
    return tgt.at[idx].add(src)

def _segment_sum(src, seg, n):
    return jax.ops.segment_sum(src, seg, n)
kernel_name = 'mk_gnn_resnorm_d4_gnn_r8_9eb4a3'

def setup_inputs(seed: int=0):
    np.random.seed(seed)
    _w = jnp.asarray

    def _rec_inputs():
        import jax
        import jax.numpy as jnp
        _gk = jax.random.key(seed)
        x = -0.000202 + 1 * jax.random.normal(jax.random.fold_in(_gk, 1), (6250, 64), jnp.float32)
        src = jax.random.randint(jax.random.fold_in(_gk, 2), (200000,), 0, 6250, jnp.int32)
        dst = jnp.minimum((6250 * jax.random.uniform(jax.random.fold_in(_gk, 3), (200000,)) ** 2.0).astype(jnp.int32), 49999)
        _o = jnp.argsort(dst, stable=True)
        src = src[_o]
        dst = dst[_o]
        edge_attr_64 = 0.000189758 + 1.00013 * jax.random.normal(jax.random.fold_in(_gk, 13), (200000, 64), jnp.float32)
        edge_weight = jax.random.uniform(jax.random.fold_in(_gk, 15), (200000,), jnp.float32, 0.0, 0.999999)
        return (x, src, dst, edge_attr_64, edge_weight)
    x, src, dst, edge_attr_64, edge_weight = _rec_inputs()

    def _L0_gnn_setup():
        import jax, jax.numpy as jnp
        import numpy as np
        LAMBDA_MAX = 2.0
        N_NODES = 12500
        N_EDGES = 200000
        D_IN = 64
        D_OUT = 64
        K = 4
        key = jax.random.key(seed)
        k1, k2, k3, k4 = jax.random.split(key, 4)
        feat = jax.random.normal(k1, (N_NODES, D_IN), dtype=jnp.float32)
        src = jax.random.randint(k2, (N_EDGES,), 0, N_NODES, dtype=jnp.int32)
        dst = jax.random.randint(k3, (N_EDGES,), 0, N_NODES, dtype=jnp.int32)
        W = jax.random.normal(k4, (K, D_IN, D_OUT), dtype=jnp.float32) * (2.0 / (D_IN + D_OUT)) ** 0.5
        b = jnp.zeros((D_OUT,), dtype=jnp.float32)
        return {'feat': feat, 'src': src, 'dst': dst, 'W': W, 'b': b}
    _L0_gnn_all = _L0_gnn_setup()
    _L0_gnn_in = {k: v for k, v in _L0_gnn_all.items() if k in ('W', 'b')}
    del _L0_gnn_all

    def _L1_gnn_setup():
        import jax, jax.numpy as jnp
        import numpy as np
        N_NODES = 6250
        N_EDGES = 100000
        N_GRAPHS = 32
        D = 64
        IN1 = 4 * D
        IN2 = 3 * D
        key = jax.random.key(seed)
        ks = jax.random.split(key, 8)
        x = jax.random.normal(ks[0], (N_NODES, D), dtype=jnp.float32)
        edge_index = jax.random.randint(ks[1], (2, N_EDGES), 0, N_NODES, dtype=jnp.int64)
        edge_attr = jax.random.normal(ks[2], (N_EDGES, D), dtype=jnp.float32)
        u = jax.random.normal(ks[3], (N_GRAPHS, D), dtype=jnp.float32)
        batch = jnp.sort(jax.random.randint(ks[4], (N_NODES,), 0, N_GRAPHS, dtype=jnp.int64))
        lim1 = 1.0 / np.sqrt(IN1)
        lim2 = 1.0 / np.sqrt(IN2)
        W1 = jax.random.uniform(ks[5], (IN1, D), jnp.float32, -lim1, lim1)
        b1 = jax.random.uniform(ks[6], (D,), jnp.float32, -lim1, lim1)
        W2 = jax.random.uniform(ks[7], (IN2, D), jnp.float32, -lim2, lim2)
        b2 = jnp.zeros((D,), jnp.float32)
        return {'x': x, 'edge_index': edge_index, 'edge_attr': edge_attr, 'u': u, 'batch': batch, 'W1': W1, 'b1': b1, 'W2': W2, 'b2': b2}
    _L1_gnn_all = _L1_gnn_setup()
    _L1_gnn_in = {k: v for k, v in _L1_gnn_all.items() if k in ('u', 'W1', 'b1', 'W2', 'b2')}
    del _L1_gnn_all

    def _L2_gnn_setup():
        import jax, jax.numpy as jnp
        import numpy as np
        C = 1.0
        SQRT_C = C ** 0.5
        EPS = 1e-07
        NUM_LAYERS = 2

        def mink(x, y):
            return jnp.sum(x * y, axis=-1, keepdims=True) - 2.0 * x[..., :1] * y[..., :1]

        def proj(x):
            sp = x[..., 1:]
            x0 = jnp.sqrt(1.0 / C + jnp.sum(sp * sp, axis=-1, keepdims=True))
            return jnp.concatenate([x0, sp], axis=-1)

        def centroid(x):
            s = jnp.mean(x, axis=0, keepdims=True)
            denom = SQRT_C * jnp.sqrt(jnp.abs(mink(s, s)) + EPS)
            return s / denom

        def logmap(p, x):
            alpha = jnp.clip(-C * mink(p, x), 1.0 + EPS, None)
            coef = jnp.arccosh(alpha) / jnp.sqrt(alpha * alpha - 1.0)
            return coef * (x - alpha * p)

        def transp(src, dst, v):
            num = C * mink(dst, v)
            den = 1.0 - C * mink(src, dst)
            return v + num / den * (src + dst)

        def expmap(p, u):
            n = jnp.sqrt(jnp.clip(mink(u, u), EPS, None))
            theta = SQRT_C * n
            return jnp.cosh(theta) * p + jnp.sinh(theta) / theta * u

        def origin(dim, dtype):
            o = jnp.zeros((1, dim), dtype=dtype)
            return o.at[0, 0].set(1.0 / SQRT_C)

        def lorentz_batchnorm(x, gamma):
            o = origin(x.shape[-1], x.dtype)
            mu = centroid(x)
            u = logmap(mu, x)
            u = transp(mu, o, u)
            var = jnp.mean(jnp.linalg.norm(u, axis=-1))
            u = u * (gamma / (var + EPS))
            u = transp(o, o, u)
            return expmap(o, u)

        def hgcn_forward(x, rows, cols, edge_weight, gamma):
            n = x.shape[0]
            h = x
            for _ in range(NUM_LAYERS):
                msg = edge_weight[:, None] * h[cols]
                h = jax.ops.segment_sum(msg, rows, num_segments=n)
                h = proj(h)
                nrm = jnp.abs(mink(h, h))
                h = h * (1.0 / jnp.sqrt(nrm)) * (1.0 / SQRT_C)
                h = lorentz_batchnorm(h, gamma)
            return h
        key = jax.random.key(seed)
        k1, k2, k3, k4 = jax.random.split(key, 4)
        N, D, E = (6250, 64, 100000)
        x = jax.random.normal(k1, (N, D), dtype=jnp.float32)
        rows = jax.random.randint(k2, (E,), 0, N, dtype=jnp.int32)
        cols = jax.random.randint(k3, (E,), 0, N, dtype=jnp.int32)
        edge_weight = jax.random.uniform(k4, (E,), dtype=jnp.float32)
        gamma = jnp.ones((1,), dtype=jnp.float32)
        return {'x': x, 'rows': rows, 'cols': cols, 'edge_weight': edge_weight, 'gamma': gamma}
    _L2_gnn_all = _L2_gnn_setup()
    _L2_gnn_in = {k: v for k, v in _L2_gnn_all.items() if k in ('gamma',)}
    del _L2_gnn_all

    def _L3_gnn_setup():
        import jax, jax.numpy as jnp
        import numpy as np
        N_NODES = 12500
        N_EDGES = 200000
        D = 64
        EPS = 1e-05
        key = jax.random.key(seed)
        k1, k2, k3, k4 = jax.random.split(key, 4)
        x = jax.random.normal(k1, (N_NODES, D), dtype=jnp.float32)
        edge_index = jax.random.randint(k2, (2, N_EDGES), 0, N_NODES, dtype=jnp.int64)
        W = jax.random.normal(k3, (D, D), dtype=jnp.float32) * (1.0 / np.sqrt(D))
        b = jnp.zeros((D,), dtype=jnp.float32)
        gamma = jnp.ones((D,), dtype=jnp.float32)
        beta = jnp.zeros((D,), dtype=jnp.float32)
        alpha = jnp.ones((D,), dtype=jnp.float32)
        return {'x': x, 'edge_index': edge_index, 'W': W, 'b': b, 'gamma': gamma, 'beta': beta, 'alpha': alpha}
    _L3_gnn_all = _L3_gnn_setup()
    _L3_gnn_in = {k: v for k, v in _L3_gnn_all.items() if k in ('W', 'b', 'gamma', 'beta', 'alpha')}
    del _L3_gnn_all
    return {'x': x, 'src': src, 'dst': dst, 'edge_attr_64': edge_attr_64, 'edge_weight': edge_weight, 'L0_gnn_W': _L0_gnn_in['W'], 'L0_gnn_b': _L0_gnn_in['b'], 'L1_gnn_u': _L1_gnn_in['u'], 'L1_gnn_W1': _L1_gnn_in['W1'], 'L1_gnn_b1': _L1_gnn_in['b1'], 'L1_gnn_W2': _L1_gnn_in['W2'], 'L1_gnn_b2': _L1_gnn_in['b2'], 'L2_gnn_gamma': _L2_gnn_in['gamma'], 'L3_gnn_W': _L3_gnn_in['W'], 'L3_gnn_b': _L3_gnn_in['b'], 'L3_gnn_gamma': _L3_gnn_in['gamma'], 'L3_gnn_beta': _L3_gnn_in['beta'], 'L3_gnn_alpha': _L3_gnn_in['alpha']}

def reference(x, src, dst, edge_attr_64, edge_weight, L0_gnn_W, L0_gnn_b, L1_gnn_u, L1_gnn_W1, L1_gnn_b1, L1_gnn_W2, L1_gnn_b2, L2_gnn_gamma, L3_gnn_W, L3_gnn_b, L3_gnn_gamma, L3_gnn_beta, L3_gnn_alpha):
    import jax
    import jax.numpy as jnp

    def _L0_gnn_ref(feat, src, dst, W, b):
        import jax, jax.numpy as jnp
        import numpy as np
        LAMBDA_MAX = 2.0
        N_NODES = 12500
        N_EDGES = 200000
        D_IN = 64
        D_OUT = 64
        K = 4
        N = feat.shape[0]
        k = W.shape[0]
        deg = jax.ops.segment_sum(jnp.ones_like(dst, dtype=feat.dtype), dst, num_segments=N)
        norm = jnp.clip(deg, 1.0) ** (-0.5)
        norm = norm[:, None]
        lam = LAMBDA_MAX

        def prop(x):
            msg = (x * norm)[src]
            return jax.ops.segment_sum(msg, dst, num_segments=N) * norm
        Tx_0 = feat
        rst = Tx_0 @ W[0]
        if k > 1:
            h = prop(Tx_0)
            Tx_1 = -2.0 * h / lam + Tx_0 * (2.0 / lam - 1.0)
            rst = rst + Tx_1 @ W[1]
            for i in range(2, k):
                h = prop(Tx_1)
                Tx_2 = -4.0 * h / lam + Tx_1 * (4.0 / lam - 2.0) - Tx_0
                rst = rst + Tx_2 @ W[i]
                Tx_0, Tx_1 = (Tx_1, Tx_2)
        return rst + b

    def _L1_gnn_ref(x, edge_index, edge_attr, u, batch, W1, b1, W2, b2):
        import jax, jax.numpy as jnp
        import numpy as np
        N_NODES = 6250
        N_EDGES = 100000
        N_GRAPHS = 32
        D = 64
        IN1 = 4 * D
        IN2 = 3 * D
        src = edge_index[0]
        dst = edge_index[1]
        edge_input = jnp.concatenate([x[src], x[dst], edge_attr, u[batch[src]]], axis=-1)
        h = jax.nn.relu(edge_input @ W1 + b1)
        agg = jax.ops.segment_sum(h, dst, num_segments=x.shape[0])
        new_input = jnp.concatenate([x, agg, u[batch]], axis=1)
        return jax.nn.relu(new_input @ W2 + b2)

    def _L2_gnn_ref(x, rows, cols, edge_weight, gamma):
        import jax, jax.numpy as jnp
        import numpy as np
        C = 1.0
        SQRT_C = C ** 0.5
        EPS = 1e-07
        NUM_LAYERS = 2

        def mink(x, y):
            return jnp.sum(x * y, axis=-1, keepdims=True) - 2.0 * x[..., :1] * y[..., :1]

        def proj(x):
            sp = x[..., 1:]
            x0 = jnp.sqrt(1.0 / C + jnp.sum(sp * sp, axis=-1, keepdims=True))
            return jnp.concatenate([x0, sp], axis=-1)

        def centroid(x):
            s = jnp.mean(x, axis=0, keepdims=True)
            denom = SQRT_C * jnp.sqrt(jnp.abs(mink(s, s)) + EPS)
            return s / denom

        def logmap(p, x):
            alpha = jnp.clip(-C * mink(p, x), 1.0 + EPS, None)
            coef = jnp.arccosh(alpha) / jnp.sqrt(alpha * alpha - 1.0)
            return coef * (x - alpha * p)

        def transp(src, dst, v):
            num = C * mink(dst, v)
            den = 1.0 - C * mink(src, dst)
            return v + num / den * (src + dst)

        def expmap(p, u):
            n = jnp.sqrt(jnp.clip(mink(u, u), EPS, None))
            theta = SQRT_C * n
            return jnp.cosh(theta) * p + jnp.sinh(theta) / theta * u

        def origin(dim, dtype):
            o = jnp.zeros((1, dim), dtype=dtype)
            return o.at[0, 0].set(1.0 / SQRT_C)

        def lorentz_batchnorm(x, gamma):
            o = origin(x.shape[-1], x.dtype)
            mu = centroid(x)
            u = logmap(mu, x)
            u = transp(mu, o, u)
            var = jnp.mean(jnp.linalg.norm(u, axis=-1))
            u = u * (gamma / (var + EPS))
            u = transp(o, o, u)
            return expmap(o, u)

        def hgcn_forward(x, rows, cols, edge_weight, gamma):
            n = x.shape[0]
            h = x
            for _ in range(NUM_LAYERS):
                msg = edge_weight[:, None] * h[cols]
                h = jax.ops.segment_sum(msg, rows, num_segments=n)
                h = proj(h)
                nrm = jnp.abs(mink(h, h))
                h = h * (1.0 / jnp.sqrt(nrm)) * (1.0 / SQRT_C)
                h = lorentz_batchnorm(h, gamma)
            return h
        return hgcn_forward(x, rows, cols, edge_weight, gamma)

    def _L3_gnn_ref(x, edge_index, W, b, gamma, beta, alpha):
        import jax, jax.numpy as jnp
        import numpy as np
        N_NODES = 12500
        N_EDGES = 200000
        D = 64
        EPS = 1e-05
        N = x.shape[0]
        src = edge_index[0]
        dst = edge_index[1]
        h = x @ W
        ones = jnp.ones(src.shape, dtype=h.dtype)
        deg = jax.ops.segment_sum(ones, dst, num_segments=N) + 1.0
        dinv = jax.lax.rsqrt(deg)
        norm = dinv[src] * dinv[dst]
        agg = jax.ops.segment_sum(h[src] * norm[:, None], dst, num_segments=N)
        agg = agg + h * (dinv * dinv)[:, None] + b
        mu = agg.mean(axis=0)
        sub = agg - alpha * mu
        var = (sub * sub).mean(axis=0)
        out = gamma * sub * jax.lax.rsqrt(var + EPS) + beta
        out = jax.nn.relu(out)
        return out + x
    edge_index = jnp.stack([src, dst])
    batch0 = jnp.zeros((6250,), jnp.int32)
    x = _layernorm(x + _L0_gnn_ref(x, src, dst, L0_gnn_W, L0_gnn_b), axis=-1)
    x = _layernorm(x + _L1_gnn_ref(x, edge_index, edge_attr_64, L1_gnn_u, batch0, L1_gnn_W1, L1_gnn_b1, L1_gnn_W2, L1_gnn_b2), axis=-1)
    x = _layernorm(x + _L2_gnn_ref(x, src, dst, edge_weight, L2_gnn_gamma), axis=-1)
    x = _layernorm(x + _L3_gnn_ref(x, edge_index, L3_gnn_W, L3_gnn_b, L3_gnn_gamma, L3_gnn_beta, L3_gnn_alpha), axis=-1)
    return x

_drawn_inputs = setup_inputs


def setup_inputs(seed=0):
    import zlib

    import numpy as np

    out = dict(_drawn_inputs(seed))
    spreads = {'L0_gnn_b': (0.0, 0.1),
     'L1_gnn_b2': (0.0, 0.1),
     'L3_gnn_b': (0.0, 0.34),
     'L3_gnn_gamma': (1.0, 0.2),
     'L3_gnn_beta': (0.0, 0.317),
     'L3_gnn_alpha': (1.0, 0.2)}
    factors = {}
    for name, (base, spread) in spreads.items():
        noise = np.random.default_rng([zlib.crc32(name.encode()), seed]).standard_normal(out[name].shape)
        drawn = base * np.exp(spread * noise) if base else spread * noise
        out[name] = jnp.asarray(drawn.astype(out[name].dtype))
    for name, factor in factors.items():
        out[name] = (out[name] * factor).astype(out[name].dtype)
    return out
```

```python
import concourse.bass as bass
from concourse import mybir
from contextlib import ExitStack

NODES, D, EDGES = 6250, 64, 200000
P = 128
CHUNKS = 8
SLAB = CHUNKS * P
RING = 4
SLABS = -(-EDGES // (SLAB * RING)) * RING
TURNS = SLABS // RING
COLS = SLABS * CHUNKS
NP = 6400
DUMP = NP - P
ALIGN = 32
WINDOWS = DUMP // ALIGN + 1
BLK, SUB = 1280, 320
BLOCKS = NP // BLK
PUB = BLK // 2
TILES = PUB // P
PASSES = ("degree", "plain", "plain", "plain", "mlp", "plain")
HI = -(-NODES // P)
GROUP = 10
KEYS = GROUP * HI
WIDE = 512
DTILES = NP // P
SPAN = 8
BATCH = 4
GROUPS = -(-NP // (GROUP * SPAN)) * SPAN
SETS = -(-GROUPS // P)
QUAD = 3
QRING = 4
KCOLS = COLS + QUAD
STREAM = 3
WAYS = -(-NODES // (STREAM * 13 * 2)) * 2
STREAMS = -(-NODES // (STREAM * WAYS))
EXACT = 256.0
FAR = 4096.0
HALF, QUART = HI * P // 2, HI * P // 16
EPS_LN, EPS_H = 1e-5, 1e-7


class Steps:

    def __init__(self):
        self.base = 0

    def stage(self, turns, *names):
        base, n = self.base, len(names)
        self.base += turns * n
        return lambda turn, name: turn * n + (base + (names.index(name) + 1 if name else 0))


def gnn_kernel(nc, xT, src, dst, weight, eaT, consts, counts, small, mats, gamma_h, out):
    BF16, F16 = mybir.dt.bfloat16, mybir.dt.float16
    F32, I32 = mybir.dt.float32, mybir.dt.int32
    ALU = mybir.AluOpType
    ACT = mybir.ActivationFunctionType
    AX = mybir.AxisListType.X
    RMAX = bass.bass_isa.ReduceOp.max
    ds = bass.ds

    ctx = ExitStack()
    with ctx:
        def sb(name, shape, dt=F32):
            return ctx.enter_context(nc.sbuf_tensor(name, shape, dt))

        def sem(name):
            return ctx.enter_context(nc.semaphore(name))

        X = sb("X", [D, NP])
        ACC_full = sb("ACC", [P, NP])
        ACC = ACC_full[0:D, :]
        T12 = sb("T12", [P, 2 * NP])
        T1 = sb("T1", [D, NP])[:]
        T2 = T12[0:D, 0:NP]
        QW = T12[:, 0:WINDOWS * D]
        NORM_full = sb("NORM", [P, NP])
        NORM = NORM_full[0:D, :]
        DINV = NORM
        DINV_kept = NORM_full[D:P, :]
        T2_kept = ACC_full[D:P, :]
        src_sb = sb("src_sb", [P, COLS], I32)
        rel = sb("rel", [P, COLS + 2 * CHUNKS])
        base_i = sb("base_i", [1, SLABS], I32)
        pos_i = sb("pos_i", [1, SLABS], I32)
        rounds_i = sb("rounds_i", [1, 1], I32)
        gathered_before = sb("gathered_before", [1, 1], I32)
        passes_before = sb("passes_before", [1, 1], I32)
        inexact_i = sb("inexact_i", [1, 1], I32)
        flags = sb("flags", [P, 4])
        roff = sb("roff", [P, 1])
        idx = sb("idx", [P, RING, CHUNKS], I32)
        WORK = sb("WORK", [P, 8192])
        oh = WORK[:, 0:2048].rearrange("p (s c n) -> p s c n", s=2, c=CHUNKS)
        ohT = WORK[:, 2048:3072]
        h_sb = WORK[:, 3072:4096].rearrange("p (s n) -> p s n", s=2)
        ea_sb = WORK[0:D, 4096:6144].rearrange("p (s n) -> p s n", s=2)
        g_sb = WORK[:, 6144:8192].rearrange("p (s n) -> p s n", s=RING)
        S = [WORK[0:D, i * BLK:(i + 1) * BLK] for i in range(6)]
        stage = WORK[0:D, 0:2 * PUB].rearrange("p (s n) -> p s n", s=2)
        rows = WORK[:, 2 * PUB:2 * PUB + NP // P * D].rearrange("p (t f) -> p t f", f=D)
        dst_i = WORK[:, 0:COLS].bitcast(I32)
        dst_f = WORK[:, 1600:1600 + COLS]
        neg = WORK[:, 3200:3200 + COLS]
        w_in = WORK[:, 6400:6400 + COLS]
        nm = WORK[:, 4800:4800 + SLABS]
        nmx = WORK[:, 5000:5000 + SLABS]
        bi = WORK[:, 5200:5200 + SLABS].bitcast(I32)
        bf = WORK[:, 5400:5400 + SLABS]
        top = WORK[:, 5600:5601]
        topx = WORK[:, 5601:5602]
        topi = WORK[:, 5602:5603].bitcast(I32)
        roundf = WORK[0:1, 5603:5604]
        lists = T12[:, 0:5 * KCOLS].rearrange("p (k c) -> p k c", k=5)
        key, low, wa, wb, wc = (T12[:, i * KCOLS:i * KCOLS + COLS] for i in range(5))
        gbase = T12[:, 7860:7860 + GROUPS]
        iota_h = T12[:, 8504:8504 + WIDE // 2].bitcast(F16)
        hot = T12[:, 8764:8764 + QUAD * WIDE // 2].bitcast(BF16).rearrange("p (s n) -> p s n", s=QUAD)
        planes = T12[:, 9788:9788 + QUAD * 4 * P // 2].bitcast(BF16).rearrange("p (s k n) -> p s k n", s=QUAD, k=4)
        quads = T12[:, 11600:11600 + QRING * 5 * QUAD].rearrange("p (s k c) -> p s k c", s=QRING, k=5)
        counts_out = ACC_full[:, 0:BATCH * WIDE].bitcast(BF16).rearrange("p (s b n) -> p s b n", s=2, b=BATCH)
        dense_out = WORK[:, 0:2 * BATCH * WIDE].rearrange("p (s b n) -> p s b n", s=2, b=BATCH)
        ranges_sb = WORK[0:1, 4200:4200 + SETS * P * 4].bitcast(I32)
        kmax, kmin, mA, mB = (ACC_full[:, i * COLS:(i + 1) * COLS] for i in range(4))
        tri, one_sq, colno, farno = (T12[:, 11000:11128], T12[:, 11128:11256], NORM_full[:, 0:COLS], NORM_full[:, COLS:2 * COLS])
        rg = T12[:, 11300:11300 + 8 * 2 * SETS]
        g_lo, g_hi, g_n, g_off, g_first, g_last, g_tot, g_set = (rg[:, i * SETS:(i + 1) * SETS] for i in range(8))
        g_all, g_allint = T12[:, 11510:11511], T12[:, 11511:11512].bitcast(I32)
        g_int = T12[:, 11500:11500 + SETS].bitcast(I32)
        rg_i = T12[:, 11400:11400 + 4 * SETS].bitcast(I32).rearrange("p (q k) -> p q k", k=4)
        src_f = NORM_full[:, 2 * COLS:3 * COLS]
        src_t = NORM_full[:, 3 * COLS:4 * COLS].bitcast(I32)
        iota_f = WORK[:, 5700:5700 + WIDE]
        part = WORK[:, 0:COLS // 2].bitcast(BF16)
        most = ACC_full[:, 4096:4096 + GROUPS]
        a_sb = T12[:, 0:STREAM * (WAYS * HI // 2)].bitcast(BF16).rearrange("p (s d h) -> p s h d", s=STREAM, h=HI)
        x12 = WORK[:, 4480:7680].bitcast(BF16).rearrange("p (t f) -> p t f", f=P)
        x3 = sb("x3", [P, HI, D], BF16)[:]
        second = WORK[0:D, 7680:7680 + STREAM * WAYS].rearrange("p (s d) -> p s d", s=STREAM)
        aw_sb = T12[:, 0:4 * (HALF // 2)].rearrange("p (s n) -> p s n", s=4)
        lt = WORK[:, 5000:5000 + 2 * D].rearrange("p (s f) -> p s f", s=2)
        cst = sb("cst", [P, 2 * P + 4 * D])
        ident, iota = cst[:, 0:P], cst[:, P:2 * P]
        ONES, MEAN, NOTIME, MINK = (cst[0:D, 2 * P + i * D:2 * P + (i + 1) * D] for i in range(4))
        ones128 = sb("ones128", [P, D])
        sm = sb("sm", [D, 16])
        (b0, u0, b1, b2, b3, g3, be3, al3, eps_c, negj, e0c, one_c, eps_h) = (sm[:, i:i + 1] for i in range(13))
        mat = sb("mat", [D, 12 * D])
        W0, W1, W2, W3, W1a, W1b, W1c, W1d, W2a, W2b, W2c, WL3 = (mat[:, i * D:(i + 1) * D] for i in range(12))
        gam = sb("gam", [D, 1])
        tiny = sb("tiny", [D, 16])
        (c1, c2, s_mean, s_sq, s_den, mu, nmu, muo, njmu, r0, var_c, sc, t_a, t_b, t_c, t_d) = (tiny[:, i:i + 1] for i in range(16))
        LA = WORK[0:D, 6 * BLK:6 * BLK + D]
        LT = WORK[0:D, 6 * BLK + D:6 * BLK + 2 * D]

        banks = ctx.enter_context(nc.psum_tensor("banks", [P, 8, 512], F32))
        A4 = banks[0:D, 0:4, 0:SUB]
        B4 = banks[0:D, 4:8, 0:SUB]

        table = nc.dram_tensor("table", [NP, D], F32).ap()
        ranges_dram = nc.dram_tensor("ranges", [SETS * P, 4], I32).ap()
        dense_w = nc.dram_tensor("dense_w", [GROUPS * KEYS, P], F32).ap()
        dense_c = nc.dram_tensor("dense_c", [P, GROUPS * KEYS], BF16).ap()
        qtable = nc.dram_tensor("qtable", [NP, D], F32).ap()

        loaded = sem("loaded")
        edges_step = sem("edges_step")
        node_step = sem("node_step")
        stage_done = sem("stage_done")
        credits = sem("credits")
        round_set = sem("round_set")
        idx_ready = sem("idx_ready")
        slabs_begun = sem("slabs_begun")
        gathered = [sem(f"gathered{u}") for u in range(RING)]
        oh_ready = sem("oh_ready")
        windows_ready = sem("windows_ready")
        slabs_free = sem("slabs_free")
        msg_ready = sem("msg_ready")
        ea_loaded = [sem(f"ea_loaded{u}") for u in range(2)]
        turned_ready = sem("turned_ready")
        ohT_ready = sem("ohT_ready")
        z_ready = sem("z_ready")
        zsum_ready = sem("zsum_ready")
        h_ready = sem("h_ready")
        range_step = sem("range_step")
        ranges_stored, ranges_loaded = sem("ranges_stored"), sem("ranges_loaded")
        quad_taken = sem("quad_taken")
        quads_begun = sem("quads_begun")
        low_ready = [sem(f"low_ready{v}") for v in range(QUAD)]
        pair_ready = [sem(f"pair_ready{v}") for v in range(QUAD)]
        pair_free = [sem(f"pair_free{v}") for v in range(QUAD)]
        group_copied = sem("group_copied")
        batch_stored = sem("batch_stored")
        batches_free = sem("batches_free")
        tile_loaded = [sem(f"tile_loaded{u}") for u in range(4)]
        kept = sem("kept")
        flag_step = sem("flag_step")
        split_step = sem("split_step")
        block_loaded = [sem(f"block_loaded{u}") for u in range(STREAM)]
        block_used = sem("block_used")
        second_ready = sem("second_ready")
        sums_taken = sem("sums_taken")
        rows_taken = sem("rows_taken")
        tile_used = sem("tile_used")
        sweep_done = sem("sweep_done")
        sweep_copied = sem("sweep_copied")
        staged = sem("staged")
        transposed = sem("transposed")
        rows_ready = sem("rows_ready")
        published = sem("published")
        q_loaded = sem("q_loaded")

        steps = Steps()
        at_setup = Steps().stage(1, "float", "pad", "negated", "slab_max", "all_max", "base_int", "base",
                                 "base_row", "base_float", "rel", "top", "all_top", "top_int", "round_count", "padded")
        at_range = Steps().stage(1, "low_i", "low", "hi_i", "hi", "key", "far", "neg", "part_a", "wa", "rest_a", "part_b", "wc",
                                 "wb", "kmax", "kmin", "positive", "last", "farno", "gbase", "iota",
                                 *[f"{n}{q}" for q in range(SETS) for n in ("below", "meets", "number", "hi", "distance", "lo")],
                                 "lo_pos", "lo_min", "one", "hi_one", "n", "n_up", "n_int", "n_quads", "quads", "before", "total", "tot", "set0",
                                 *[f"set{q}" for q in range(1, SETS)], "all", "off_a", "first", "end", "four", "delta", "turns",
                                 "int0", "int1", "int2", "turns_up", "turns_int", "turns_set")
        at_deg = steps.stage(BLOCKS, "deg1", "deg0", "root0", "root1", "norm", "dinv")
        at_cheb = [steps.stage(1, *names) for names in (("scaled",), ("scaled", "done"), ("scaled", "done"))]
        at_flag = Steps().stage(1, "most", "all_most", "many", "thrice", "passes", "inexact_int", "passes_int", "rounds")
        at_split = Steps().stage(4, "first", "rest1", "second", "rest2", "third")
        LN = ("mean", "centred", "squared", "var", "std", "inverse", "out")
        at_ln0 = steps.stage(BLOCKS, "product", "sum", *LN)
        at_c = steps.stage(1, "c1", "c1b", "c2", "c2b")
        at_P = steps.stage(2 * BLOCKS, "product")
        at_Q = steps.stage(2 * BLOCKS, "product")
        at_ln1 = steps.stage(BLOCKS, "product", "relu", "sum", *LN)
        at_m = []
        for _ in range(2):
            at_m.append((
                steps.stage(BLOCKS, "squared", "space", "root0", "inverse0", "quotient", "twice", "time", "squared2", "mink", "abs", "root", "inverse", "out"),
                steps.stage(1, "sum", "mean", "square", "mink", "abs", "root", "inverse", "mu", "nmu", "muo", "njmu",
                            "LA", "den0", "inv0", "zero", "LT"),
                steps.stage(BLOCKS, "alpha", "clip", "plus", "square", "root", "arg", "ln", "inverse", "coef", "diff",
                            "tangent", "time", "moved", "squared", "norm2", "norm"),
                steps.stage(1, "sum", "mean", "inverse", "scale"),
                steps.stage(BLOCKS, "scaled", "row0", "squared", "mink", "clip", "theta", "exp", "expinv", "diff",
                            "thetainv", "sinhc", "zc", "p0", "p1", "p2", "p3", "blend", "mask", "masked", "chosen",
                            "space", "cosh", "out"),
            ))
        at_ln2 = steps.stage(BLOCKS, "sum", *LN)
        at_lin = steps.stage(BLOCKS, "product", "out")
        at_l3 = steps.stage(1, "sum_scaled", "self1", "self2", "agg", "bias", "sum", "mu", "sub", "sq", "var", "std",
                            "inverse", "scale", "out", "plus")
        at_ln3 = steps.stage(BLOCKS, "sum", *LN)

        def barrier(eng, n):
            eng.drain().then_inc(stage_done, 1)
            eng.wait_ge(stage_done, 5 * n)

        def begin(eng, at, i):
            if at(i, None):
                eng.wait_ge(node_step, at(i, None))

        def blk(t, i):
            return t[:, ds(i * BLK, BLK)]

        def sub(t, i, j):
            return t[:, ds(i * BLK + j * SUB, SUB)]

        def four(t):
            return t.rearrange("p (j n) -> p j n", j=4)

        def blk4(t, i):
            return four(blk(t, i))

        def quads_of(eng, g, n):
            bounds = ((0, GROUPS * COLS), (1, GROUPS * COLS), (-QUAD * GROUPS * COLS, COLS))
            return [eng.value_load(ranges_sb[0:1, ds(g * 4 + k, 1)], min_val=bounds[k][0], max_val=bounds[k][1]) for k in range(n)]

        def column_of(eng, q, delta):
            return nc.s_assert_within(eng.snap(q * QUAD + delta), 0, COLS - 1, skip_runtime_bounds_check_because="the ranges were made so")

        def before(eng, p, R):
            if PASSES[p] == "mlp":
                GB = eng.value_load(gathered_before[0:1, 0:1], min_val=0, max_val=3 * P)
                return GB + R, eng.value_load(passes_before[0:1, 0:1], min_val=1, max_val=4), GB
            return R * p, p, R * max(p - 1, 0)

        def slab_no(RB, r, i, u):
            return (r + RB) * SLABS + i * RING + u

        def one_hots_before(p, RB, R, r):
            if PASSES[p] == "mlp":
                return RB * (SLABS + 1) + r * (SLABS + 2)
            return (r + RB) * (SLABS + 1) + R if p > PASSES.index("mlp") else (r + RB) * (SLABS + 1)

        def inexact_of(eng):
            return eng.value_load(inexact_i[0:1, 0:1], min_val=0, max_val=1)

        block = ctx.enter_context(nc.Block())

        @block.sync
        def _(sp):
            for to, of in ((dst_i, dst), (src_sb[:], src), (w_in, weight), (cst[:], consts), (X[:], xT),
                           (sm[:], small), (mat[:], mats), (gam[:], gamma_h), (colno, counts[:, 0:COLS]),
                           (tri, counts[:, COLS:COLS + P]), (one_sq, counts[:, COLS + P:COLS + 2 * P]),
                           (g_first, counts[:, COLS + 2 * P:COLS + 2 * P + SETS]), (iota_f, counts[:, COLS + 2 * P + SETS:])):
                sp.dma_start(to, of).then_inc(loaded, 16)
            count = [0, 0]

            def end():
                count[0] += 1
                barrier(sp, count[0])

            def blocks_of_counts(k):
                with sp.If(inexact == 0):
                    with sp.Fori(0, STREAMS) as i:
                        for u in range(STREAM):
                            sp.wait_ge(block_used, i * STREAM + (k * STREAMS * STREAM + u + 1))
                            sp.dma_start(a_sb[:, u, :, :].rearrange("p h d -> p d h"),
                                         dense_c[:, ds((i * STREAM + u) * (WAYS * HI), WAYS * HI)].rearrange("l (d h) -> l d h", h=HI))\
                              .then_inc(block_loaded[u], 16)
                end()

            def keep(to, of, n):
                sp.dma_start(to, of).then_inc(kept, 16)
                sp.wait_ge(kept, 16 * n)

            def publish(k, where, keeping=None):
                if keeping:
                    keep(*keeping)
                sp.wait_ge(rows_ready, 2 * BLOCKS * (k + 1))
                if where is None:
                    pass
                elif where is out:
                    full = NODES // P
                    sp.dma_start(out[0:full * P, :].rearrange("(t p) f -> p t f", p=P), rows[:, 0:full, :]).then_inc(published, 16)
                    sp.dma_start(out[full * P:NODES, :], rows[0:NODES - full * P, full, :]).then_inc(published, 16)
                    count[1] += 32
                else:
                    sp.dma_start(where.rearrange("(t p) f -> p t f", p=P), rows).then_inc(published, 16)
                    count[1] += 16
                if where is not None:
                    sp.wait_ge(published, count[1])
                end()

            sp.wait_ge(range_step, at_range(0, "turns_set"))
            sp.dma_start(ranges_dram.rearrange("(q p) k -> p q k", p=P), rg_i).then_inc(ranges_stored, 16)
            sp.wait_ge(ranges_stored, 16)
            sp.dma_start(ranges_sb, ranges_dram.rearrange("(a g) k -> a (g k)", a=1)).then_inc(ranges_loaded, 16)
            sp.wait_ge(ranges_loaded, 16)
            end()
            with sp.Fori(0, GROUPS // (2 * BATCH)) as i:
                for u in range(2):
                    sp.wait_ge(group_copied, i * (2 * BATCH) + (u + 1) * BATCH + 2)
                    batch = dense_w[ds((i * 2 + u) * (BATCH * KEYS), BATCH * KEYS), :].rearrange("(b k) l -> b k l", b=BATCH)
                    full = KEYS // 4
                    sp.dma_start(batch[:, 0:full * 4, :].rearrange("b (m j) l -> m b (j l)", j=4), dense_out[0:full, u, :, :]).then_inc(batch_stored, 16)
                    sp.dma_start(batch[:, full * 4:KEYS, :].rearrange("(a b) k l -> a b (k l)", a=1),
                                 dense_out[full:full + 1, u, :, 0:(KEYS - full * 4) * P]).then_inc(batch_stored, 16)
                    sp.dma_start(dense_c[:, ds((i * 2 + u) * (BATCH * KEYS), BATCH * KEYS)].rearrange("l (b k) -> l b k", b=BATCH),
                                 counts_out[:, u, :, 0:KEYS]).then_inc(batch_stored, 16)
                    sp.wait_ge(batch_stored, i * 96 + (u + 1) * 48)
                    sp.sem_inc(batches_free, 1)
            end()
            R = sp.value_load(rounds_i[0:1, 0:1], min_val=1, max_val=P)
            end()
            end()
            inexact = inexact_of(sp)
            for k in range(3):
                publish(k, table, ((DINV_kept, T1[:], 1), None, (T2_kept, ACC, 2))[k])
                blocks_of_counts(k)
                if k == 2:
                    keep(T2, T2_kept, 3)
                end()
            end()
            keep(DINV[:], DINV_kept, 4)
            end()
            publish(3, table)
            publish(4, qtable)
            row = qtable[0:P, :]
            windows = bass.AP(tensor=row.tensor, offset=row.offset, ap=[[D, P], [ALIGN * D, WINDOWS], [1, D]])
            sp.dma_start(QW.rearrange("p (j f) -> p j f", f=D), windows).then_inc(q_loaded, 16)
            sp.wait_ge(q_loaded, 16)
            end()
            RB, _, GB = before(sp, 4, R)
            with sp.Fori(0, R) as r:
                with sp.Fori(0, TURNS) as i:
                    for u in range(RING):
                        sp.wait_ge(slabs_free, slab_no(RB, r, i, u) + 1 + (RING - 2))
                        sp.dma_start(ea_sb[:, u % 2, :], eaT[ds(i * RING + u, 1), :, :].rearrange("a f e -> f (a e)"))\
                          .then_inc(ea_loaded[u % 2], 16)
            end()
            end()
            for l in range(2):
                publish(5 + l, None)
                for sw in range(2):
                    with sp.Fori(0, DTILES // 2) as i:
                        for u in range(4):
                            sp.wait_ge(tile_used, i * 4 + ((2 * l + sw) * 2 * DTILES + u + 1))
                            sp.dma_start(aw_sb[:, u, :], dense_w[0:NP * HI, :].rearrange("(d h) l -> d (h l)", h=HI)[
                                ds(i * (2 * P) + u // 2 * P, P), sw * HALF + u % 2 * (HALF // 2):sw * HALF + (u % 2 + 1) * (HALF // 2)])\
                              .then_inc(tile_loaded[u], 16)
                end()
                for _ in range(5):
                    end()
            end()
            end()
            publish(7, table)
            blocks_of_counts(3)
            end()
            end()
            publish(8, out)

        @block.gpsimd
        def _(pool):
            count = [0]

            def end():
                count[0] += 1
                barrier(pool, count[0])

            pool.wait_ge(edges_step, at_setup(0, "slab_max"))
            nc.gpsimd.partition_all_reduce(nmx, nm, P, RMAX).then_inc(edges_step, 1)
            pool.wait_ge(edges_step, at_setup(0, "top"))
            nc.gpsimd.partition_all_reduce(topx, top, P, RMAX).then_inc(edges_step, 1)
            pool.wait_ge(range_step, at_range(0, "wb"))
            nc.gpsimd.partition_all_reduce(kmax, key, P, RMAX).then_inc(range_step, 1)
            nc.gpsimd.partition_all_reduce(kmin, neg, P, RMAX).then_inc(range_step, 1)
            pool.sem_inc(slabs_free, RING)
            pool.sem_inc(transposed, 2)
            for v in range(QUAD):
                pool.sem_inc(pair_free[v], 1)
            pool.sem_inc(pair_ready[QUAD - 1], QRING)
            pool.sem_inc(group_copied, 2)
            pool.sem_inc(batches_free, 2)
            pool.sem_inc(tile_used, 4)
            pool.sem_inc(block_used, STREAM)
            pool.sem_inc(sums_taken, STREAM)
            end()
            def take(q, g, col):
                slot = q & (QRING - 1)
                pool.wait_ge(pair_ready[QUAD - 1], q + 1)
                pool.sem_inc(quads_begun, 1)
                nc.gpsimd.tensor_copy(quads[:, ds(slot, 1), 1:5, :].rearrange("p s k c -> p (s k) c"), lists[:, 1:5, ds(col, QUAD)])
                nc.gpsimd.tensor_tensor(quads[:, ds(slot, 1), 0, :].rearrange("p s c -> p (s c)"), lists[:, 0, ds(col, QUAD)],
                                        gbase[:, ds(g, 1)].to_broadcast([P, QUAD]), ALU.subtract).then_inc(quad_taken, 1)

            with pool.Fori(0, GROUPS) as g:
                first, past, delta = quads_of(pool, g, 3)
                with pool.Fori(first, past) as q:
                    take(q, g, column_of(pool, q, delta))
            _, past = quads_of(pool, GROUPS - 1, 2)
            for k in range(QRING - 1):
                take(pool.snap(past + k, min_val=0, max_val=GROUPS * COLS), 0, 0)
            end()
            R = pool.value_load(rounds_i[0:1, 0:1], min_val=1, max_val=P)

            def gathers(p):
                RB, _, GB = before(pool, p, R)
                with pool.Fori(0, R) as r:
                    with pool.Fori(0, TURNS) as i:
                        for u in range(RING):
                            pool.wait_ge(slabs_free, slab_no(RB, r, i, u) + 1)
                            nc.gpsimd.tensor_copy(idx[:, u, :], src_sb[:, ds((i * RING + u) * CHUNKS, CHUNKS)]).then_inc(idx_ready, 1)
                            pool.wait_ge(idx_ready, slab_no(GB, r, i, u) + 1)
                            pool.sem_inc(slabs_begun, 1)
                            for c in range(CHUNKS):
                                nc.gpsimd.indirect_dma_start(
                                    out=g_sb[:, u, c * D:(c + 1) * D], out_offset=None, in_=table,
                                    in_offset=bass.IndirectOffsetOnAxis(ap=idx[:, u, c:c + 1], axis=0)).then_inc(gathered[u], 16)

            pool.wait_ge(flag_step, at_flag(0, "most"))
            nc.gpsimd.partition_all_reduce(flags[:, 1:2], flags[:, 0:1], P, RMAX).then_inc(flag_step, 1)
            end()
            end()
            inexact = inexact_of(pool)
            for k in range(3):
                end()
                with pool.If(inexact > 0):
                    gathers(1 + k)
                end()
                end()
            end()
            end()
            end()
            end()
            end()
            gathers(4)
            end()
            end()
            for l in range(2):
                end()
                end()
                for _ in range(5):
                    end()
            end()
            end()
            end()
            with pool.If(inexact > 0):
                gathers(5)
            end()
            end()
            end()
            end()

        @block.vector
        def _(dve):
            V = nc.vector
            count = [0]

            def end():
                count[0] += 1
                barrier(dve, count[0])

            def did(ins):
                ins.then_inc(node_step, 1)

            def setup():
                at = lambda name: dve.wait_ge(edges_step, at_setup(0, name))
                fin = lambda ins: ins.then_inc(edges_step, 1)
                dve.wait_ge(loaded, 16 * 13)
                fin(V.tensor_copy(dst_f, dst_i))
                at("float")
                fin(V.tensor_scalar(neg, dst_f, 0.0, -1e6, ALU.is_lt, ALU.mult))
                at("pad")
                fin(V.scalar_tensor_tensor(neg, dst_f, -1.0, neg, ALU.mult, ALU.add))
                at("negated")
                fin(V.tensor_reduce(nm, neg.rearrange("p (s c) -> p s c", c=CHUNKS), AX, ALU.max))
                at("all_max")
                fin(V.tensor_scalar(bi, nmx, -1.0, None, ALU.mult))
                at("base_int")
                fin(V.tensor_scalar(bi, bi, -ALIGN, None, ALU.bitwise_and))
                at("base")
                fin(V.tensor_copy(base_i[:], bi[0:1, :]))
                fin(V.tensor_copy(bf, bi))
                at("base_float")
                wide = bf.unsqueeze(2).to_broadcast([P, SLABS, CHUNKS])
                fin(V.tensor_tensor(rel[:, 0:COLS].rearrange("p (s c) -> p s c", c=CHUNKS),
                                    dst_f.rearrange("p (s c) -> p s c", c=CHUNKS), wide, ALU.subtract))
                at("rel")
                fin(V.tensor_reduce(top, rel[:, 0:COLS], AX, ALU.max))
                at("all_top")
                fin(V.tensor_copy(topi, topx))
                at("top_int")
                fin(V.tensor_scalar(rounds_i[:], topi[0:1, :], 7, None, ALU.arith_shift_right))
                at("round_count")
                V.memset(rel[:, COLS:COLS + 2 * CHUNKS], -1.0)
                V.memset(ones128[:], 1.0)
                fin(V.tensor_scalar(rounds_i[:], rounds_i[:], 1.0, None, ALU.add))

            def ranges():
                at = lambda name: dve.wait_ge(range_step, at_range(0, name))
                fin = lambda ins: ins.then_inc(range_step, 1)
                fin(V.tensor_scalar(src_t, src_sb[:], P - 1, None, ALU.bitwise_and))
                at("low_i")
                fin(V.tensor_copy(low, src_t))
                V.memset(lists[:, 1:5, COLS:KCOLS], 0.0)
                V.memset(lists[:, 0, COLS:KCOLS], -1.0)
                V.memset(rg_i[:], 0)
                at("low")
                fin(V.tensor_scalar(src_t, src_sb[:], 7, None, ALU.arith_shift_right))
                at("hi_i")
                fin(V.tensor_copy(src_f, src_t))
                at("hi")
                fin(V.scalar_tensor_tensor(key, dst_f, float(HI), src_f, ALU.mult, ALU.add))
                at("key")
                fin(V.tensor_scalar(neg, dst_f, 0.0, -1e6, ALU.is_lt, ALU.mult))
                at("far")
                fin(V.scalar_tensor_tensor(neg, key, -1.0, neg, ALU.mult, ALU.add))
                fin(V.tensor_copy(part, w_in))
                at("part_a")
                fin(V.tensor_copy(wa, part))
                at("wa")
                fin(V.tensor_tensor(wb, w_in, wa, ALU.subtract))
                at("rest_a")
                fin(V.tensor_copy(part, wb))
                at("part_b")
                fin(V.tensor_tensor(wc, wb, part, ALU.subtract))
                at("wc")
                fin(V.tensor_copy(wb, part))
                at("kmin")
                fin(V.tensor_scalar(kmin, kmin, -1.0, None, ALU.mult))
                fin(V.tensor_scalar(g_last, g_first, float(KEYS - 1), None, ALU.add))
                fin(V.tensor_scalar(farno, colno, -1.0, FAR, ALU.mult, ALU.add))
                fin(V.tensor_scalar(gbase, colno[:, 0:GROUPS], float(KEYS), None, ALU.mult))
                fin(V.tensor_copy(iota_h, iota_f))
                at("iota")
                for q in range(SETS):
                    col = slice(q, q + 1)
                    fin(V.tensor_scalar(mA, kmin, g_last[:, col], None, ALU.is_le))
                    at(f"below{q}")
                    fin(V.scalar_tensor_tensor(mB, kmax, g_first[:, col], mA, ALU.is_ge, ALU.mult))
                    at(f"meets{q}")
                    fin(V.scalar_tensor_tensor(mA, colno, 1.0, mB, ALU.add, ALU.mult))
                    at(f"number{q}")
                    fin(V.tensor_reduce(g_hi[:, col], mA, AX, ALU.max))
                    at(f"hi{q}")
                    fin(V.tensor_tensor(mA, farno, mB, ALU.mult))
                    at(f"distance{q}")
                    fin(V.tensor_reduce(g_lo[:, col], mA, AX, ALU.max))
                    at(f"lo{q}")
                fin(V.tensor_scalar(g_lo, g_lo, -1.0, FAR, ALU.mult, ALU.add))
                at("lo_pos")
                fin(V.tensor_scalar(g_lo, g_lo, float(COLS - 1), None, ALU.min))
                at("lo_min")
                fin(V.tensor_scalar(g_n, g_lo, 1.0, None, ALU.add))
                at("one")
                fin(V.tensor_tensor(g_hi, g_hi, g_n, ALU.max))
                at("hi_one")
                fin(V.tensor_tensor(g_n, g_hi, g_lo, ALU.subtract))
                at("n")
                fin(V.tensor_scalar(g_n, g_n, float(QUAD - 1), float(-(-2 ** 14 // QUAD)), ALU.add, ALU.mult))
                at("n_up")
                fin(V.tensor_copy(g_int, g_n))
                at("n_int")
                fin(V.tensor_scalar(g_int, g_int, 14, None, ALU.arith_shift_right))
                at("n_quads")
                fin(V.tensor_copy(g_n, g_int))
                at("total")
                fin(V.tensor_copy(g_tot, banks[:, 1, 0:SETS]))
                fin(V.memset(g_set, 0.0))
                for q in range(1, SETS):
                    at(f"set{q - 1}")
                    fin(V.tensor_tensor(g_set[:, q:q + 1], g_set[:, q - 1:q], g_tot[:, q - 1:q], ALU.add))
                at(f"set{SETS - 1}")
                fin(V.tensor_tensor(g_all, g_set[:, SETS - 1:SETS], g_tot[:, SETS - 1:SETS], ALU.add))
                fin(V.tensor_copy(g_off, banks[:, 0, 0:SETS]))
                at("off_a")
                fin(V.tensor_tensor(g_off, g_off, g_set, ALU.add))
                at("first")
                fin(V.tensor_tensor(g_tot, g_off, g_n, ALU.add))
                fin(V.tensor_scalar(g_hi, g_off, -float(QUAD), None, ALU.mult))
                at("four")
                fin(V.tensor_tensor(g_lo, g_lo, g_hi, ALU.add))
                at("delta")
                fin(V.tensor_scalar(g_all, g_all, float(QRING - 1 - (SETS * P - GROUPS)), None, ALU.add))
                for k, v in enumerate((g_off, g_tot, g_lo)):
                    fin(V.tensor_copy(rg_i[:, :, k], v))
                at("turns")
                fin(V.tensor_copy(g_allint, g_all))
                at("turns_up")
                fin(V.tensor_scalar(g_allint, g_allint, QRING.bit_length() - 1, None, ALU.arith_shift_right))
                at("turns_int")
                fin(V.tensor_copy(rg_i[0:1, 0, 3:4], g_allint[0:1, :]))

            def build_dense():
                turns = dve.value_load(ranges_sb[0:1, 3:4], min_val=GROUPS // QRING, max_val=GROUPS * COLS // QRING)
                with dve.Fori(0, turns) as i:
                    for s in range(QRING):
                        now = dve.snap(i * QRING + (s + 1), min_val=1, max_val=GROUPS * COLS)
                        dve.wait_ge(quad_taken, now)
                        for v in range(QUAD):
                            q_key, q_low, *q_w = (quads[:, s, k, v:v + 1] for k in range(5))
                            dve.wait_ge(pair_free[v], now)
                            V.tensor_scalar(planes[:, v, 0, :], iota_h[:, 0:P], q_low, None, ALU.is_equal).then_inc(low_ready[v], 1)
                            last = V.tensor_scalar(hot[:, v, :], iota_h, q_key, None, ALU.is_equal)
                            dve.wait_ge(low_ready[v], now)
                            for k in range(3):
                                last = V.tensor_scalar(planes[:, v, 1 + k, :], planes[:, v, 0, :], q_w[k], None, ALU.mult)
                            last.then_inc(pair_ready[v], 1)
                end()

            def dense_pass(l):
                V.memset(ACC[:, 2 * HALF:NP], 0.0)
                for sw in range(2):
                    dve.wait_ge(tile_used, 4 + (2 * l + sw + 1) * 2 * DTILES)
                    V.tensor_copy(ACC[:, sw * HALF:(sw + 1) * HALF].rearrange("p (j n) -> p j n", j=8), banks[0:D, :, 0:QUART]).then_inc(sweep_copied, 1)
                end()

            def edge_pass(p, R):
                kind = PASSES[p]
                RB, PB, GB = before(dve, p, R)
                V.memset(ACC[:], 0.0).then_inc(round_set, 1)
                V.memset(roff[:], 0.0).then_inc(round_set, 1)
                V.tensor_copy(pos_i[:], base_i[:]).then_inc(round_set, 1)

                def one_hots(first, slot):
                    for c in range(CHUNKS):
                        last = V.tensor_scalar(oh[:, slot, c, :], iota, roff[:], rel[:, ds(first + c, 1)], ALU.add, ALU.is_equal)
                    last.then_inc(oh_ready, 1)

                with dve.Fori(0, R) as r:
                    dve.wait_ge(round_set, (RB + r) * 2 + (PB * 3 + 3))
                    ahead = 2 if kind == "mlp" else 1
                    for k in range(ahead):
                        one_hots(k * CHUNKS, k)
                    with dve.Fori(0, TURNS) as i:
                        for u in range(RING):
                            n = slab_no(RB, r, i, u)
                            pos = dve.value_load(pos_i[0:1, ds(i * RING + u, 1)], min_val=0, max_val=DUMP)
                            if kind == "mlp":
                                dve.wait_ge(z_ready, (r * SLABS + i * RING + u) + 1)
                                dve.wait_ge(gathered[u], ((GB + r) * TURNS + i + 1) * (16 * CHUNKS))
                                V.tensor_tensor(h_sb[:, u % 2, :], banks[:, 2 + u % 2, :], g_sb[:, u, :], ALU.add).then_inc(zsum_ready, 1)
                            else:
                                one_hots((i * RING + u + 1) * CHUNKS, (u + 1) % 2)
                            dve.wait_ge(windows_ready, n + 1)
                            dve.wait_ge(slabs_free, n + RING)
                            V.tensor_tensor(ACC[:, ds(pos, P)], ACC[:, ds(pos, P)], banks[0:D, u % 2, 0:P], ALU.add).then_inc(slabs_free, 1)
                            if kind == "mlp":
                                one_hots((i * RING + u + 2) * CHUNKS, u % 2)
                    dve.wait_ge(oh_ready, one_hots_before(p, RB, R, r) + (SLABS + ahead))
                    if kind == "mlp":
                        dve.wait_ge(turned_ready, (r + 1) * (SLABS + 1))
                    V.tensor_scalar(roff[:], roff[:], float(P), None, ALU.add).then_inc(round_set, 1)
                    V.tensor_scalar(pos_i[:], pos_i[:], float(P), float(DUMP), ALU.add, ALU.min).then_inc(round_set, 1)

            def set_flag():
                at = lambda name: dve.wait_ge(flag_step, at_flag(0, name))
                fin = lambda ins: ins.then_inc(flag_step, 1)
                fin(V.tensor_reduce(flags[:, 0:1], most, AX, ALU.max))
                at("all_most")
                fin(V.tensor_scalar(flags[:, 2:3], flags[:, 1:2], EXACT, None, ALU.is_gt))
                at("many")
                fin(V.tensor_scalar(flags[:, 3:4], flags[:, 2:3], 3.0, 1.0, ALU.mult, ALU.add))
                fin(V.tensor_copy(roundf, rounds_i[:]))
                at("passes")
                fin(V.tensor_copy(inexact_i[:], flags[0:1, 2:3]))
                fin(V.tensor_copy(passes_before[:], flags[0:1, 3:4]))
                fin(V.scalar_tensor_tensor(gathered_before[:], flags[0:1, 3:4], 1.0, roundf, ALU.subtract, ALU.mult))

            def counts_pass(k):
                at = lambda name: dve.wait_ge(split_step, at_split(k, name))
                fin = lambda ins: ins.then_inc(split_step, 1)
                V.memset(ACC[:, STREAMS * STREAM * WAYS:NP], 0.0)
                fin(V.tensor_copy(x12[:, :, 0:D], rows))
                at("first")
                fin(V.tensor_tensor(rows, rows, x12[:, :, 0:D], ALU.subtract))
                at("rest1")
                fin(V.tensor_copy(x12[:, :, D:P], rows))
                at("second")
                fin(V.tensor_tensor(rows, rows, x12[:, :, D:P], ALU.subtract))
                at("rest2")
                fin(V.tensor_copy(x3, rows[:, 0:HI, :]))
                with dve.Fori(0, STREAMS) as i:
                    for u in range(STREAM):
                        n = i * STREAM + (k * STREAMS * STREAM + u)
                        dve.wait_ge(second_ready, n + 1)
                        V.tensor_tensor(ACC[:, ds((i * STREAM + u) * WAYS, WAYS)], second[:, u, :], banks[0:D, u, 0:WAYS], ALU.add).then_inc(sums_taken, 1)

            def plain_pass(k, p, R):
                with dve.If(inexact > 0):
                    edge_pass(p, R)
                with dve.Else():
                    counts_pass(k)
                end()

            def publish(k, make):
                for i in range(BLOCKS):
                    for u in range(2):
                        dve.wait_ge(transposed, i * 2 + (2 * BLOCKS * k + u + 1))
                        make(i, u, stage[:, u, :], ds(i * BLK + u * PUB, PUB)).then_inc(staged, 1)
                end()

            def scaled(a, b):
                return lambda i, u, to, cols: V.tensor_tensor(to, a[:, cols], b[:, cols], ALU.mult)

            def plain(a):
                return lambda i, u, to, cols: V.tensor_copy(to, a[:, cols])

            def product(at, bias):
                def make(i, u, to, cols):
                    dve.wait_ge(node_step, at(i * 2 + u, "product"))
                    of = banks[0:D, 2 * u:2 * u + 2, 0:SUB]
                    to = to.rearrange("p (j n) -> p j n", j=2)
                    return V.tensor_copy(to, of) if bias is None else V.tensor_scalar(to, of, bias, None, ALU.add)
                return make

            def layer_norm(at, first):
                for i in range(BLOCKS):
                    w = lambda name: dve.wait_ge(node_step, at(i, name))
                    first(i, w)
                    w("mean")
                    did(V.tensor_tensor(blk4(ACC, i), blk4(ACC, i), A4, ALU.subtract))
                    w("std")
                    did(V.reciprocal(S[1], S[1]))
                    w("inverse")
                    did(V.tensor_tensor(blk(X, i), blk(ACC, i), S[1], ALU.mult))
                end()

            setup()
            ranges()
            end()
            build_dense()
            R = dve.value_load(rounds_i[0:1, 0:1], min_val=1, max_val=P)
            set_flag()
            dve.wait_ge(flag_step, at_flag(0, "rounds"))
            edge_pass(0, R)
            end()
            for i in range(BLOCKS):
                w = lambda name: dve.wait_ge(node_step, at_deg(i, name))
                begin(dve, at_deg, i)
                did(V.tensor_scalar(S[0], blk(ACC, i), 1.0, None, ALU.max))
                did(V.tensor_scalar(S[1], blk(ACC, i), 1.0, None, ALU.add))
                w("root1")
                did(V.reciprocal(blk(NORM, i), S[0]))
                did(V.reciprocal(blk(T1, i), S[1]))
            end()
            inexact = inexact_of(dve)
            for k, (of, factor, last, to) in enumerate(((X[:], -1.0, None, T1[:]), (T1[:], -2.0, X[:], ACC), (ACC, -2.0, T1[:], ACC))):
                publish(k, scaled(of, NORM))
                plain_pass(k, 1 + k, R)
                w = lambda name: dve.wait_ge(node_step, at_cheb[k](0, name))
                did(V.scalar_tensor_tensor(to, ACC, factor, NORM, ALU.mult, ALU.mult))
                if last is not None:
                    w("scaled")
                    did(V.tensor_tensor(to, to, last, ALU.subtract))
                end()

            def first0(i, w):
                w("product")
                did(V.scalar_tensor_tensor(blk4(ACC, i), A4, b0, blk4(X, i), ALU.add, ALU.add))

            layer_norm(at_ln0, first0)
            dve.wait_ge(node_step, at_c(0, "c1"))
            did(V.tensor_tensor(c1, banks[0:D, 0, 0:1], b1, ALU.add))
            dve.wait_ge(node_step, at_c(0, "c2"))
            did(V.tensor_tensor(c2, banks[0:D, 0, 0:1], b2, ALU.add))
            end()
            publish(3, product(at_P, None))
            publish(4, product(at_Q, c1))
            end()
            edge_pass(4, R)
            end()

            def first1(i, w):
                w("relu")
                did(V.tensor_tensor(blk(ACC, i), S[2], blk(X, i), ALU.add))

            layer_norm(at_ln1, first1)
            for l in range(2):
                publish(5 + l, plain(X if l == 0 else T1))
                dense_pass(l)
                a1, a2, a3, a4, a5 = at_m[l]
                for i in range(BLOCKS):
                    w = lambda name: dve.wait_ge(node_step, a1(i, name))
                    w("root0")
                    did(V.reciprocal(S[3][0:1, :], S[2][0:1, :]))
                    w("inverse0")
                    did(V.scalar_tensor_tensor(four(S[3][0:1, :]), banks[0:1, 0:4, 0:SUB], 1.0, four(S[3][0:1, :]), ALU.add, ALU.mult))
                    w("quotient")
                    did(V.tensor_tensor(S[3][0:1, :], S[3][0:1, :], S[2][0:1, :], ALU.add))
                    w("twice")
                    did(V.tensor_scalar(ACC[0:1, ds(i * BLK, BLK)], S[3][0:1, :], 0.5, None, ALU.mult))
                    w("root")
                    did(V.reciprocal(S[1], S[1]))
                    w("inverse")
                    did(V.tensor_tensor(blk(ACC, i), blk(ACC, i), S[1], ALU.mult))
                end()
                w = lambda name: dve.wait_ge(node_step, a2(0, name))
                did(V.tensor_reduce(s_mean, ACC[:, 0:NODES], AX, ALU.add))
                w("sum")
                did(V.tensor_scalar(s_mean, s_mean, 1.0 / NODES, None, ALU.mult))
                w("mean")
                did(V.tensor_tensor(s_sq, s_mean, s_mean, ALU.mult))
                w("root")
                did(V.reciprocal(s_den, s_den))
                w("inverse")
                did(V.tensor_tensor(mu, s_mean, s_den, ALU.mult))
                w("mu")
                did(V.tensor_scalar(nmu, mu, -1.0, None, ALU.mult))
                did(V.tensor_tensor(muo, mu, e0c, ALU.add))
                did(V.tensor_tensor(njmu, mu, negj, ALU.mult))
                w("njmu")
                did(V.tensor_scalar(LA, ONES, njmu, None, ALU.mult))
                did(V.tensor_scalar(r0[0:1, :], mu[0:1, :], -1.0, -1.0, ALU.mult, ALU.add))
                w("den0")
                did(V.reciprocal(r0[0:1, :], r0[0:1, :]))
                did(V.memset(LT, 0.0))
                w("zero")
                did(V.tensor_scalar(LT[0:1, :], ONES[0:1, :], r0[0:1, :], None, ALU.mult))
                end()
                for i in range(BLOCKS):
                    w = lambda name: dve.wait_ge(node_step, a3(i, name))
                    w("alpha")
                    did(V.tensor_scalar(four(S[1]), A4, 1.0 + EPS_H, None, ALU.max))
                    w("clip")
                    did(V.tensor_scalar(S[2], S[1], 1.0, None, ALU.add))
                    w("plus")
                    did(V.scalar_tensor_tensor(S[3], S[1], 1.0, S[2], ALU.subtract, ALU.mult))
                    w("root")
                    did(V.tensor_tensor(S[2], S[1], S[3], ALU.add))
                    w("ln")
                    did(V.reciprocal(S[3], S[3]))
                    w("inverse")
                    did(V.tensor_tensor(S[2], S[2], S[3], ALU.mult))
                    w("coef")
                    did(V.scalar_tensor_tensor(S[4], S[1], nmu, blk(ACC, i), ALU.mult, ALU.add))
                    w("diff")
                    did(V.tensor_tensor(blk(ACC, i), S[4], S[2], ALU.mult))
                    w("time")
                    did(V.scalar_tensor_tensor(blk4(ACC, i), B4, muo, blk4(ACC, i), ALU.mult, ALU.add))
                end()
                w = lambda name: dve.wait_ge(node_step, a4(0, name))
                did(V.tensor_reduce(var_c, T2[:, 0:NODES], AX, ALU.add))
                w("sum")
                did(V.tensor_scalar(var_c, var_c, 1.0 / NODES, EPS_H, ALU.mult, ALU.add))
                w("mean")
                did(V.reciprocal(var_c, var_c))
                w("inverse")
                did(V.tensor_tensor(sc, var_c, gam[:], ALU.mult))
                end()
                for i in range(BLOCKS):
                    w = lambda name: dve.wait_ge(node_step, a5(i, name))
                    begin(dve, a5, i)
                    did(V.tensor_scalar(blk(ACC, i), blk(ACC, i), sc, None, ALU.mult))
                    w("scaled")
                    did(V.scalar_tensor_tensor(ACC[0:1, ds(i * BLK, BLK)], ACC[0:1, ds(i * BLK, BLK)], -1.0,
                                               ACC[0:1, ds(i * BLK, BLK)], ALU.mult, ALU.add))
                    w("mink")
                    did(V.tensor_scalar(four(S[1]), A4, EPS_H, None, ALU.max))
                    w("exp")
                    did(V.reciprocal(S[4], S[3]))
                    w("expinv")
                    did(V.tensor_tensor(S[5], S[3], S[4], ALU.subtract))
                    w("diff")
                    did(V.reciprocal(S[2], S[2]))
                    w("thetainv")
                    did(V.scalar_tensor_tensor(S[5], S[5], 0.5, S[2], ALU.mult, ALU.mult))
                    did(V.tensor_scalar(S[0], S[1], 1.0, None, ALU.min))
                    w("zc")
                    did(V.tensor_scalar(S[2], S[0], 1.0 / 362880, None, ALU.mult))
                    w("p0")
                    did(V.scalar_tensor_tensor(S[2], S[2], 1.0 / 5040, S[0], ALU.add, ALU.mult))
                    w("p1")
                    did(V.scalar_tensor_tensor(S[2], S[2], 1.0 / 120, S[0], ALU.add, ALU.mult))
                    w("p2")
                    did(V.scalar_tensor_tensor(S[2], S[2], 1.0 / 6, S[0], ALU.add, ALU.mult))
                    w("p3")
                    did(V.scalar_tensor_tensor(S[2], S[2], 1.0, S[5], ALU.add, ALU.subtract))
                    did(V.tensor_scalar(S[1], S[1], 1.0, None, ALU.is_lt))
                    w("mask")
                    did(V.tensor_tensor(S[2], S[2], S[1], ALU.mult))
                    w("masked")
                    did(V.tensor_tensor(S[5], S[5], S[2], ALU.add))
                    w("chosen")
                    did(V.tensor_tensor(blk(T1, i), blk(ACC, i), S[5], ALU.mult))
                    did(V.tensor_tensor(S[4][0:1, :], S[3][0:1, :], S[4][0:1, :], ALU.add))
                    w("cosh")
                    did(V.scalar_tensor_tensor(T1[0:1, ds(i * BLK, BLK)], S[4][0:1, :], 0.5,
                                               T1[0:1, ds(i * BLK, BLK)], ALU.mult, ALU.add))
                end()

            layer_norm(at_ln2, lambda i, w: begin(dve, at_ln2, i) or did(V.tensor_tensor(blk(ACC, i), blk(T1, i), blk(X, i), ALU.add)))
            end()
            publish(7, scaled(T1, DINV))
            plain_pass(3, 5, R)
            w = lambda name: dve.wait_ge(node_step, at_l3(0, name))
            did(V.tensor_tensor(ACC[:], ACC[:], DINV[:], ALU.mult))
            did(V.tensor_tensor(T2, T1, DINV[:], ALU.mult))
            w("self1")
            did(V.tensor_tensor(T2, T2, DINV[:], ALU.mult))
            w("self2")
            did(V.tensor_tensor(ACC[:], ACC[:], T2, ALU.add))
            w("agg")
            did(V.tensor_scalar(ACC[:], ACC[:], b3, None, ALU.add))
            w("bias")
            did(V.tensor_reduce(t_a, ACC[:, 0:NODES], AX, ALU.add))
            w("sum")
            did(V.tensor_scalar(t_a, t_a, 1.0 / NODES, al3, ALU.mult, ALU.mult))
            w("mu")
            did(V.tensor_scalar(ACC[:], ACC[:], t_a, None, ALU.subtract))
            w("sq")
            did(V.tensor_scalar(t_b, t_b, 1.0 / NODES, None, ALU.mult))
            w("std")
            did(V.reciprocal(t_b, t_b))
            w("inverse")
            did(V.tensor_tensor(t_c, t_b, g3, ALU.mult))
            w("out")
            did(V.tensor_tensor(ACC[:], T2, X[:], ALU.add))
            end()
            layer_norm(at_ln3, lambda i, w: begin(dve, at_ln3, i) or did(V.tensor_tensor(blk(ACC, i), blk(ACC, i), blk(X, i), ALU.add)))
            publish(8, plain(X))

        @block.scalar
        def _(act):
            C = nc.scalar
            count = [0]

            def end():
                count[0] += 1
                barrier(act, count[0])

            def did(ins):
                ins.then_inc(node_step, 1)

            def publish(k):
                for i in range(BLOCKS):
                    for u in range(2):
                        act.wait_ge(transposed, i * 2 + (2 * BLOCKS * k + u + 1 + 2))
                        C.activation(rows[:, ds(i * 2 * TILES + u * TILES, TILES), :],
                                     banks[:, 6 + u, 0:TILES * D].rearrange("p (t f) -> p t f", f=D), ACT.Copy).then_inc(rows_ready, 1)
                end()

            def layer_norm(at, first=None):
                for i in range(BLOCKS):
                    w = lambda name: act.wait_ge(node_step, at(i, name))
                    if first:
                        first(i, w)
                    w("centred")
                    did(C.activation(S[0], blk(ACC, i), ACT.Square))
                    w("var")
                    did(C.activation(four(S[1]), B4, ACT.Sqrt, bias=eps_c))
                end()

            end()
            with act.Fori(0, GROUPS // (2 * BATCH)) as i:
                for u in range(2 * BATCH):
                    b = u % BATCH
                    _, past = quads_of(act, i * (2 * BATCH) + u, 2)
                    if b == 0:
                        act.wait_ge(batches_free, i * 2 + (u // BATCH + 1))
                    act.wait_ge(pair_free[QUAD - 1], past + 1)
                    C.activation(dense_out[:, u // BATCH, b, :], banks[:, u % 2, :], ACT.Copy)
                    C.activation(counts_out[:, u // BATCH, b, :], banks[:, 2 + u % 2, :], ACT.Copy,
                                 accum_out=most[:, ds(i * (2 * BATCH) + u, 1)]).then_inc(group_copied, 1)
            end()
            R = act.value_load(rounds_i[0:1, 0:1], min_val=1, max_val=P)
            end()
            for i in range(BLOCKS):
                act.wait_ge(node_step, at_deg(i, "deg0"))
                did(C.activation(S[0], S[0], ACT.Sqrt))
                did(C.activation(S[1], S[1], ACT.Sqrt))
            end()
            inexact = inexact_of(act)

            def plain_pass(k):
                with act.If(inexact == 0):
                    with act.Fori(0, STREAMS) as i:
                        for u in range(STREAM):
                            n = i * STREAM + (k * STREAMS * STREAM + u)
                            act.wait_ge(block_used, n + (STREAM + 1))
                            C.activation(second[:, u, :], banks[D:P, u, 0:WAYS], ACT.Copy).then_inc(second_ready, 1)
                end()

            for k in range(3):
                publish(k)
                plain_pass(k)
                end()
            layer_norm(at_ln0)
            end()
            publish(3)
            publish(4)
            end()
            def turned(k):
                act.wait_ge(turned_ready, k)
                C.activation(ohT[:, 0:512], banks[:, 4, :], ACT.Copy)
                C.activation(ohT[:, 512:1024], banks[:, 5, :], ACT.Copy).then_inc(ohT_ready, 1)

            with act.Fori(0, R) as r:
                turned(r * (SLABS + 1) + 1)
                with act.Fori(0, TURNS) as i:
                    for u in range(RING):
                        act.wait_ge(zsum_ready, r * SLABS + i * RING + (u + 1))
                        C.activation(h_sb[:, u % 2, :], h_sb[:, u % 2, :], ACT.Relu).then_inc(h_ready, 1)
                        turned(r * (SLABS + 1) + i * RING + (u + 2))
            end()

            def first1(i, w):
                w("product")
                did(C.activation(four(S[2]), A4, ACT.Relu, bias=c2))

            layer_norm(at_ln1, first1)
            for l in range(2):
                publish(5 + l)
                for sw in range(2):
                    with act.Fori(0, DTILES // 2) as i:
                        for v in range(2):
                            act.wait_ge(tile_used, i * 4 + ((2 * l + sw) * 2 * DTILES + 2 * v + 2))
                            C.activation(lt[:, v, :], rows[:, ds(i * 2 + v, 1), :], ACT.Copy).then_inc(rows_taken, 1)
                end()
                a1, a2, a3, a4, a5 = at_m[l]
                for i in range(BLOCKS):
                    w = lambda name: act.wait_ge(node_step, a1(i, name))
                    begin(act, a1, i)
                    did(C.activation(S[0], blk(ACC, i), ACT.Square))
                    w("space")
                    did(C.activation(four(S[2][0:1, :]), banks[0:1, 0:4, 0:SUB], ACT.Sqrt, bias=one_c[0:1, :]))
                    w("time")
                    did(C.activation(S[0], blk(ACC, i), ACT.Square))
                    w("mink")
                    did(C.activation(four(S[1]), B4, ACT.Abs))
                    w("abs")
                    did(C.activation(S[1], S[1], ACT.Sqrt))
                end()
                act.wait_ge(node_step, a2(0, "mink"))
                did(C.activation(s_den, banks[0:D, 0, 0:1], ACT.Abs))
                act.wait_ge(node_step, a2(0, "abs"))
                did(C.activation(s_den, s_den, ACT.Sqrt, bias=eps_h))
                end()
                for i in range(BLOCKS):
                    w = lambda name: act.wait_ge(node_step, a3(i, name))
                    w("square")
                    did(C.activation(S[3], S[3], ACT.Sqrt))
                    w("arg")
                    did(C.activation(S[2], S[2], ACT.Ln))
                    w("moved")
                    did(C.activation(S[0], blk(ACC, i), ACT.Square))
                    w("norm2")
                    did(C.activation(blk4(T2, i), A4, ACT.Sqrt))
                end()
                end()
                for i in range(BLOCKS):
                    w = lambda name: act.wait_ge(node_step, a5(i, name))
                    w("row0")
                    did(C.activation(S[0], blk(ACC, i), ACT.Square))
                    w("clip")
                    did(C.activation(S[2], S[1], ACT.Sqrt))
                    w("theta")
                    did(C.activation(S[3], S[2], ACT.Exp))
                end()
            layer_norm(at_ln2)
            for i in range(BLOCKS):
                act.wait_ge(node_step, at_lin(i, "product"))
                did(C.activation(blk4(T1, i), A4, ACT.Copy))
            end()
            publish(7)
            plain_pass(3)
            w = lambda name: act.wait_ge(node_step, at_l3(0, name))
            w("sub")
            did(C.activation(T2[:, 0:NODES], ACC[:, 0:NODES], ACT.Square, accum_out=t_b))
            w("var")
            did(C.activation(t_b, t_b, ACT.Sqrt, bias=eps_c))
            w("scale")
            did(C.activation(T2, ACC[:], ACT.Relu, bias=be3, scale=t_c))
            end()
            layer_norm(at_ln3)
            publish(8)

        @block.tensor
        def _(pe):
            T = nc.tensor
            count = [0]

            def end():
                count[0] += 1
                barrier(pe, count[0])

            def did(ins):
                ins.then_inc(node_step, 1)

            def edge_pass(p, R):
                kind = PASSES[p]
                RB, _, GB = before(pe, p, R)

                def turn(slot):
                    for c in range(CHUNKS):
                        last = T.transpose(banks[:, 4 + c // 4, c % 4 * P:(c % 4 + 1) * P], oh[:, slot, c, :], ident)
                    last.then_inc(turned_ready, 1)

                with pe.Fori(0, R) as r:
                    made = one_hots_before(p, RB, R, r)
                    if kind == "mlp":
                        pe.wait_ge(oh_ready, made + 1)
                        turn(0)
                    with pe.Fori(0, TURNS) as i:
                        for u in range(RING):
                            n = slab_no(RB, r, i, u)
                            m = r * SLABS + i * RING + u
                            if kind == "mlp":
                                pos = pe.value_load(pos_i[0:1, ds(i * RING + u, 1)], min_val=0, max_val=DUMP)
                                pe.wait_ge(ohT_ready, r * (SLABS + 1) + i * RING + (u + 1))
                                pe.wait_ge(ea_loaded[u % 2], (r * (SLABS // 2) + i * (RING // 2) + (u // 2 + 1)) * 16)
                                for c in range(CHUNKS):
                                    z = banks[:, 2 + u % 2, c * D:(c + 1) * D]
                                    T.matmul(z, ohT[:, c * P:(c + 1) * P], QW[:, ds(pos * (D // ALIGN), D)], start=True, stop=False)
                                    last = T.matmul(z, ea_sb[:, u % 2, c * P:(c + 1) * P], W1c, start=False, stop=True)
                                last.then_inc(z_ready, 1)
                                pe.wait_ge(oh_ready, made + (i * RING + (u + 2)))
                                turn((u + 1) % 2)
                                pe.wait_ge(h_ready, m + 1)
                            else:
                                pe.wait_ge(oh_ready, made + (i * RING + (u + 1)))
                            if kind == "plain":
                                pe.wait_ge(gathered[u], ((GB + r) * TURNS + i + 1) * (16 * CHUNKS))
                            pe.wait_ge(slabs_free, n + 1 + (RING - 2))
                            for c in range(CHUNKS):
                                of = (ones128[:] if kind == "degree" else
                                      (g_sb[:, u, c * D:(c + 1) * D] if kind == "plain" else h_sb[:, u % 2, c * D:(c + 1) * D]))
                                last = T.matmul(banks[0:D, u % 2, 0:P], of, oh[:, u % 2, c, :], start=c == 0, stop=c == CHUNKS - 1)
                            last.then_inc(windows_ready, 1)
                    if kind == "mlp":
                        pe.wait_ge(ohT_ready, (r + 1) * (SLABS + 1))

            def counts_pass(k):
                pe.wait_ge(split_step, at_split(k, "third"))
                with pe.Fori(0, STREAMS) as i:
                    for u in range(STREAM):
                        n = i * STREAM + (k * STREAMS * STREAM + u)
                        pe.wait_ge(sums_taken, n + 1)
                        pe.wait_ge(block_loaded[u], i * 16 + (k * STREAMS + 1) * 16)
                        for t in range(HI):
                            T.matmul(banks[:, u, 0:WAYS], x12[:, t, :], a_sb[:, u, t, :], start=t == 0, stop=False, skip_group_check=True)
                            last = T.matmul(banks[0:D, u, 0:WAYS], x3[:, t, :], a_sb[:, u, t, :], start=False, stop=t == HI - 1, skip_group_check=True)
                        last.then_inc(block_used, 1)

            def plain_pass(k, p, R):
                with pe.If(inexact > 0):
                    edge_pass(p, R)
                with pe.Else():
                    counts_pass(k)
                end()

            def build_dense():
                def quad(q, u, begins):
                    now = pe.snap(q + 1, min_val=1, max_val=GROUPS * COLS)
                    for v in range(QUAD):
                        keys = hot[:, v, :].rearrange("p (m j) -> p j m", j=WIDE // P)
                        if v == QUAD - 1:
                            now = pe.snap(now + QRING, min_val=QRING + 1, max_val=GROUPS * COLS)
                        pe.wait_ge(pair_ready[v], now)
                        T.matmul(banks[:, 2 + u, :], planes[:, v, 0, :], hot[:, v, :], start=begins and v == 0, stop=False, skip_group_check=True)
                        for j in range(WIDE // P):
                            for k in range(3):
                                last = T.matmul(banks[:, u, j * P:(j + 1) * P], keys[:, j, :], planes[:, v, 1 + k, :],
                                                start=begins and v == 0 and j == 0 and k == 0, stop=False, skip_group_check=True)
                        last.then_inc(pair_free[v], 1)

                with pe.Fori(0, GROUPS // SPAN) as i:
                    first, = quads_of(pe, i * SPAN, 1)
                    past = quads_of(pe, i * SPAN + (SPAN - 1), 2)[1]
                    with pe.If(past < first + (SPAN + 1)):
                        for u in range(SPAN):
                            pe.wait_ge(group_copied, i * SPAN + (u + 1))
                            quad(first + u, u % 2, True)
                    with pe.Else():
                        with pe.Fori(0, SPAN // 2) as j:
                            for u in range(2):
                                first, past = quads_of(pe, i * SPAN + j * 2 + u, 2)
                                pe.wait_ge(group_copied, i * SPAN + j * 2 + (u + 1))
                                quad(first, u, True)
                                with pe.If(past > first + 1):
                                    with pe.Fori(first + 1, past) as q:
                                        quad(q, u, False)
                for v in range(QUAD):
                    pe.drain().then_inc(pair_free[v], QRING - 1)
                end()

            def dense_pass(l):
                def tiles(sw, i, first):
                    for u in range(4):
                        if u % 2 == 0:
                            pe.wait_ge(rows_taken, i * 2 + ((2 * l + sw) * DTILES + u // 2 + 1))
                        pe.wait_ge(tile_loaded[u], i * 16 + ((2 * l + sw) * (DTILES // 2) + 1) * 16)
                        for j in range(4):
                            last = T.matmul(banks[0:D, u % 2 * 4 + j, 0:QUART], lt[:, u // 2, :], aw_sb[:, u, j * QUART:(j + 1) * QUART],
                                            start=first and u < 2, stop=False, skip_group_check=True)
                        last.then_inc(tile_used, 1)

                for sw in range(2):
                    if l or sw:
                        pe.wait_ge(sweep_copied, 2 * l + sw)
                    tiles(sw, 0, True)
                    with pe.Fori(1, DTILES // 2) as i:
                        tiles(sw, i, False)
                end()

            def publish(k, before=None):
                for i in range(BLOCKS):
                    for u in range(2):
                        v = i * 2 + (2 * BLOCKS * k + u + 1)
                        if before:
                            before(i, u)
                        pe.wait_ge(staged, v)
                        if i > 0:
                            pe.wait_ge(rows_ready, v - 2)
                        for t in range(TILES):
                            last = T.transpose(banks[:, 6 + u, t * D:(t + 1) * D], stage[:, u, t * P:(t + 1) * P], ident[0:D, 0:D])
                        last.then_inc(transposed, 1)
                end()

            def product(at, W):
                def before(i, u):
                    for j in range(2):
                        last = T.matmul(banks[0:D, 2 * u + j, 0:SUB], W, X[:, ds(i * BLK + u * PUB + j * SUB, SUB)], start=True, stop=True)
                    did(last)
                return before

            def times(to, W, of, start=True, stop=True):
                for j in range(4):
                    last = T.matmul(to[:, j, :], W, of(j), start=start, stop=stop)
                return last

            def many(to, i, pairs):
                for j in range(4):
                    for k, (W, a) in enumerate(pairs):
                        last = T.matmul(to[:, j, :], W, sub(a, i, j), start=k == 0, stop=k == len(pairs) - 1)
                return last

            def s_of(k):
                return lambda j: S[k][:, j * SUB:(j + 1) * SUB]

            def layer_norm(at, pairs=None):
                for i in range(BLOCKS):
                    w = lambda name: pe.wait_ge(node_step, at(i, name))
                    if pairs:
                        begin(pe, at, i)
                        did(many(A4, i, pairs))
                    w("sum")
                    did(times(A4, MEAN, lambda j: sub(ACC, i, j)))
                    w("squared")
                    did(times(B4, MEAN, s_of(0)))
                end()

            pe.wait_ge(range_step, at_range(0, "quads"))
            T.matmul(banks[:, 0, 0:SETS], tri, g_n, start=True, stop=True).then_inc(range_step, 1)
            T.matmul(banks[:, 1, 0:SETS], one_sq, g_n, start=True, stop=True).then_inc(range_step, 1)
            end()
            build_dense()
            R = pe.value_load(rounds_i[0:1, 0:1], min_val=1, max_val=P)
            edge_pass(0, R)
            end()
            end()
            inexact = inexact_of(pe)
            for k in range(3):
                publish(k)
                plain_pass(k, 1 + k, R)
                end()
            layer_norm(at_ln0, ((W0, X), (W1, T1), (W2, T2), (W3, ACC)))
            did(T.matmul(banks[0:D, 0, 0:1], W1d, u0, start=True, stop=True))
            pe.wait_ge(node_step, at_c(0, "c1b"))
            did(T.matmul(banks[0:D, 0, 0:1], W2c, u0, start=True, stop=True))
            end()
            publish(3, product(at_P, W1a))
            publish(4, product(at_Q, W1b))
            end()
            edge_pass(4, R)
            end()
            layer_norm(at_ln1, ((W2a, X), (W2b, ACC)))
            for l in range(2):
                publish(5 + l)
                dense_pass(l)
                a1, a2, a3, a4, a5 = at_m[l]
                for i in range(BLOCKS):
                    w = lambda name: pe.wait_ge(node_step, a1(i, name))
                    w("squared")
                    did(times(A4, NOTIME, s_of(0)))
                    w("squared2")
                    did(times(B4, MINK, s_of(0)))
                end()
                pe.wait_ge(node_step, a2(0, "square"))
                did(T.matmul(banks[0:D, 0, 0:1], MINK, s_sq, start=True, stop=True))
                end()
                for i in range(BLOCKS):
                    w = lambda name: pe.wait_ge(node_step, a3(i, name))
                    begin(pe, a3, i)
                    did(times(A4, LA, lambda j: sub(ACC, i, j)))
                    w("tangent")
                    did(times(B4, LT, lambda j: sub(ACC, i, j)))
                    w("squared")
                    did(times(A4, ONES, s_of(0)))
                end()
                end()
                for i in range(BLOCKS):
                    w = lambda name: pe.wait_ge(node_step, a5(i, name))
                    w("squared")
                    did(times(A4, MINK, s_of(0)))
                end()
            layer_norm(at_ln2)
            for i in range(BLOCKS):
                if_first = at_lin(i, "product")
                did(times(A4, WL3, lambda j: sub(X, i, j)))
                pe.wait_ge(node_step, if_first + 1)
            end()
            publish(7)
            plain_pass(3, 5, R)
            end()
            layer_norm(at_ln3)
            publish(8)


def kernel(**inputs):
    import numpy as np
    import concourse.bacc as bacc
    from concourse.bass_utils import run_bass_kernel_spmd as run

    a = {k: np.asarray(v) for k, v in inputs.items()}
    f32 = np.float32

    def columns(v, fill):
        padded = np.full(SLABS * SLAB, fill, v.dtype)
        padded[:EDGES] = v
        return np.ascontiguousarray(padded.reshape(COLS, P).T)

    xT = np.zeros((D, NP), f32)
    xT[:, :NODES] = a["x"].T
    ea = np.zeros((SLABS * SLAB, D), f32)
    ea[:EDGES] = a["edge_attr_64"]
    eaT = np.ascontiguousarray(ea.reshape(SLABS, SLAB, D).transpose(0, 2, 1))

    ones = np.ones((D, D), f32)
    notime, mink, e0 = ones.copy(), ones.copy(), np.zeros((D, D), f32)
    notime[0], mink[0], e0[0] = 0, -1, 1
    consts = np.zeros((P, 2 * P + 4 * D), f32)
    consts[:, :P] = np.eye(P)
    consts[:, P:2 * P] = np.arange(P)
    consts[:D, 2 * P:] = np.concatenate([ones, ones / D, notime, mink], 1)

    counts = np.zeros((P, COLS + 2 * P + SETS + WIDE), f32)
    counts[:, :COLS] = np.arange(COLS)
    counts[:, COLS:COLS + P] = np.triu(np.ones((P, P)), 1)
    counts[:, COLS + P:COLS + 2 * P] = 1
    counts[:, COLS + 2 * P:COLS + 2 * P + SETS] = KEYS * (np.arange(P)[:, None] + P * np.arange(SETS))
    counts[:, COLS + 2 * P + SETS:] = np.arange(WIDE)

    small = np.zeros((D, 16), f32)
    for i, v in enumerate((a["L0_gnn_b"], a["L1_gnn_u"][0], a["L1_gnn_b1"], a["L1_gnn_b2"], a["L3_gnn_b"],
                           a["L3_gnn_gamma"], a["L3_gnn_beta"], a["L3_gnn_alpha"])):
        small[:, i] = v
    small[:, 8] = EPS_LN
    small[:, 9] = -mink[:, 0]
    small[:, 10] = e0[:, 0]
    small[:, 11] = 1
    small[:, 12] = EPS_H
    W1, W2 = a["L1_gnn_W1"], a["L1_gnn_W2"]
    mats = np.concatenate([*a["L0_gnn_W"], *W1.reshape(4, D, D), *W2.reshape(3, D, D), a["L3_gnn_W"]], 1)
    arrays = {
        "xT": xT, "src": columns(a["src"], 0), "dst": columns(a["dst"], -1), "weight": columns(a["edge_weight"], 0),
        "eaT": eaT, "consts": consts, "counts": counts, "small": small, "mats": np.ascontiguousarray(mats),
        "gamma_h": np.ascontiguousarray(np.broadcast_to(a["L2_gnn_gamma"], (D, 1))),
    }
    nc = bacc.Bacc("TRN2", target_bir_lowering=False, num_devices=1)
    aps = {k: nc.dram_tensor("in_" + k, v.shape, mybir.dt.from_np(v.dtype), kind="ExternalInput").ap() for k, v in arrays.items()}
    out = nc.dram_tensor("out", (NODES, D), mybir.dt.float32, kind="ExternalOutput").ap()
    gnn_kernel(nc, **aps, out=out)
    r = run(nc, [{"in_" + k: v for k, v in arrays.items()}], core_ids=[0])
    return r.results[0]["out"]
```
